# Optimizing a Trainium2 kernel written in Bass

```python
import numpy as np
import jax
import jax.numpy as jnp

def _softmax(x, axis=-1):
    return jax.nn.softmax(x, axis=axis)

def _gelu(x):
    return jax.nn.gelu(x, approximate=True)

def _silu(x):
    return jax.nn.silu(x)

def _sigmoid(x):
    return jax.nn.sigmoid(x)

def _layernorm(x, axis=-1, eps=1e-05):
    m = jnp.mean(x, axis=axis, keepdims=True)
    v = jnp.var(x, axis=axis, keepdims=True)
    return (x - m) / jnp.sqrt(v + eps)

def _scatter_add(tgt, idx, src, axis=0):
    return tgt.at[idx].add(src)

def _segment_sum(src, seg, n):
    return jax.ops.segment_sum(src, seg, n)
kernel_name = 'mk_xattn_ffn_d2_seqx_r8_38605a'

def setup_inputs(seed: int=0):
    np.random.seed(seed)
    _w = jnp.asarray

    def _rec_inputs():
        import jax
        import jax.numpy as jnp
        _rk = jax.random.key(seed)
        x = -0.000125 + 0.9999 * jax.random.normal(jax.random.fold_in(_rk, 1), (4, 256, 256), jnp.float32)
        _lenS = 256 - jax.random.randint(jax.random.fold_in(_rk, 7), (4,), 0, max(1, 256 // 4) + 1, jnp.int32)
        _lenS2 = 1601 - jax.random.randint(jax.random.fold_in(_rk, 8), (4,), 0, max(1, 1601 // 4) + 1, jnp.int32)
        _ctx_2048P = jax.random.normal(jax.random.fold_in(_rk, 11), (4, 16, 256), jnp.float32)
        _ctx_2048c = jax.random.dirichlet(jax.random.fold_in(_rk, 511), 0.3 * jnp.ones((16,), jnp.float32), (4, 1601))
        _ctx_2048t = jnp.einsum('bsk,bkd->bsd', _ctx_2048c, _ctx_2048P)
        _ctx_2048t = _ctx_2048t * jax.lax.rsqrt(jnp.mean(jnp.square(_ctx_2048t)) + 1e-12) * 0.953939
        ctx_2048 = -0.000514642 + 1.00011 * (_ctx_2048t + 0.3 * jax.random.normal(jax.random.fold_in(_rk, 611), (4, 1601, 256), jnp.float32))
        _validS = jnp.arange(256)[None, :] < _lenS[:, None]
        _validS2 = jnp.arange(1601)[None, :] < _lenS2[:, None]
        _causal = jnp.tril(jnp.ones((256, 256), dtype=bool))
        mask_BxS2_bk0 = jnp.logical_not(jnp.broadcast_to(_validS2[:, :], (4, 1601)))
        return (x, ctx_2048, mask_BxS2_bk0)
    x, ctx_2048, mask_BxS2_bk0 = _rec_inputs()

    def _L0_xattn_setup():
        import jax, jax.numpy as jnp
        import numpy as np
        key = jax.random.key(seed)
        k1, k2, k3 = jax.random.split(key, 3)
        B, S, D, M = (8, 256, 256, 128)
        hidden_states = jax.random.normal(k1, (B, S, D), dtype=jnp.float32)
        memory_tokens = jax.random.normal(k2, (B, M, D), dtype=jnp.float32)
        memory_mask = jax.random.randint(k3, (B, M), 0, 2).astype(jnp.bool_)
        return {'hidden_states': hidden_states, 'memory_tokens': memory_tokens, 'memory_mask': memory_mask}
    _L0_xattn_all = _L0_xattn_setup()
    _L0_xattn_in = {k: v for k, v in _L0_xattn_all.items() if k in ()}
    del _L0_xattn_all

    def _L0_ffn_setup():
        import jax, jax.numpy as jnp
        import numpy as np
        B, T, D = (4, 256, 256)
        E = 8
        K = 2
        F = 1024 // (E // 2)
        key = jax.random.key(seed)
        ks = jax.random.split(key, 5)
        s_in = 1.0 / np.sqrt(D)
        s_mid = 1.0 / np.sqrt(F)
        x = jax.random.normal(ks[0], (B, T, D), dtype=jnp.float32)
        Wr = jax.random.normal(ks[1], (D, E), dtype=jnp.float32) * s_in
        Wg = jax.random.normal(ks[2], (E, D, F), dtype=jnp.float32) * s_in
        Wu = jax.random.normal(ks[3], (E, D, F), dtype=jnp.float32) * s_in
        Wd = jax.random.normal(ks[4], (E, F, D), dtype=jnp.float32) * s_mid
        return {'x': x, 'Wr': Wr, 'Wg': Wg, 'Wu': Wu, 'Wd': Wd}
    _L0_ffn_all = _L0_ffn_setup()
    _L0_ffn_in = {k: v for k, v in _L0_ffn_all.items() if k in ('Wr', 'Wg', 'Wu', 'Wd')}
    del _L0_ffn_all

    def _L1_xattn_setup():
        import jax, jax.numpy as jnp
        import numpy as np
        key = jax.random.key(seed)
        k = jax.random.split(key, 6)
        B, S, D, NKV = (4, 512, 256, 64)
        inv = D ** (-0.5)
        return {'x': jax.random.normal(k[0], (B, S, D), jnp.float32), 'W_qkv': jax.random.normal(k[1], (3 * D, D), jnp.float32) * inv, 'W_o': jax.random.normal(k[2], (D, D), jnp.float32) * inv, 'beta_q': jnp.array(1.0, jnp.float32), 'beta_k': jnp.array(1.0, jnp.float32), 'gate': jnp.array(0.0, jnp.float32), 'log_tau': jnp.array(0.0, jnp.float32), 'K_mem': jax.random.normal(k[3], (B, NKV, D), jnp.float32), 'V_mem': jax.random.normal(k[4], (B, NKV, D), jnp.float32), 'clip_k': 54}
    _L1_xattn_all = _L1_xattn_setup()
    _L1_xattn_in = {k: v for k, v in _L1_xattn_all.items() if k in ('W_qkv', 'W_o', 'beta_q', 'beta_k', 'gate', 'log_tau')}
    del _L1_xattn_all

    def _L1_ffn_setup():
        import jax, jax.numpy as jnp
        import numpy as np
        EPS = 1e-05

        def activation_quant(x):
            scale = 127.0 / jnp.clip(jnp.max(jnp.abs(x), axis=-1, keepdims=True), EPS, None)
            return jnp.clip(jnp.round(x * scale), -128.0, 127.0) / scale

        def weight_quant(w):
            scale = 1.0 / jnp.clip(jnp.mean(jnp.abs(w)), EPS, None)
            return jnp.clip(jnp.round(w * scale), -1.0, 1.0) / scale

        def bitlinear(x, w):
            xq = x + jax.lax.stop_gradient(activation_quant(x) - x)
            wq = w + jax.lax.stop_gradient(weight_quant(w) - w)
            return jnp.einsum('bsd,hd->bsh', xq, wq)
        key = jax.random.key(seed)
        k1, k2, k3 = jax.random.split(key, 3)
        B, S, D, H = (4, 256, 256, 1024)
        x = jax.random.normal(k1, (B, S, D), dtype=jnp.float32)
        w1 = jax.random.normal(k2, (H, D), dtype=jnp.float32) * 0.02
        w2 = jax.random.normal(k3, (D, H), dtype=jnp.float32) * 0.02
        return {'x': x, 'w1': w1, 'w2': w2}
    _L1_ffn_all = _L1_ffn_setup()
    _L1_ffn_in = {k: v for k, v in _L1_ffn_all.items() if k in ('w1', 'w2')}
    del _L1_ffn_all
    return {'x': x, 'ctx_2048': ctx_2048, 'mask_BxS2_bk0': mask_BxS2_bk0, 'L0_ffn_Wr': _L0_ffn_in['Wr'], 'L0_ffn_Wg': _L0_ffn_in['Wg'], 'L0_ffn_Wu': _L0_ffn_in['Wu'], 'L0_ffn_Wd': _L0_ffn_in['Wd'], 'L1_xattn_W_qkv': _L1_xattn_in['W_qkv'], 'L1_xattn_W_o': _L1_xattn_in['W_o'], 'L1_xattn_beta_q': _L1_xattn_in['beta_q'], 'L1_xattn_beta_k': _L1_xattn_in['beta_k'], 'L1_xattn_gate': _L1_xattn_in['gate'], 'L1_xattn_log_tau': _L1_xattn_in['log_tau'], 'L1_ffn_w1': _L1_ffn_in['w1'], 'L1_ffn_w2': _L1_ffn_in['w2']}

def reference(x, ctx_2048, mask_BxS2_bk0, L0_ffn_Wr, L0_ffn_Wg, L0_ffn_Wu, L0_ffn_Wd, L1_xattn_W_qkv, L1_xattn_W_o, L1_xattn_beta_q, L1_xattn_beta_k, L1_xattn_gate, L1_xattn_log_tau, L1_ffn_w1, L1_ffn_w2):
    import jax
    import jax.numpy as jnp

    def _L0_xattn_ref(hidden_states, memory_tokens, memory_mask):
        import jax, jax.numpy as jnp
        import numpy as np
        B, S, D = hidden_states.shape
        scale = 1.0 / jnp.sqrt(jnp.asarray(D, hidden_states.dtype))
        scores = jnp.einsum('bsd,bmd->bsm', hidden_states, memory_tokens) * scale
        neg_inf = jnp.asarray(-1e+30, scores.dtype)
        scores = jnp.where(memory_mask[:, None, :], scores, neg_inf)
        attn = jax.nn.softmax(scores, axis=-1)
        readout = jnp.einsum('bsm,bmd->bsd', attn, memory_tokens)
        valid_b = jnp.any(memory_mask, axis=-1)
        out = jnp.where(valid_b[:, None, None], readout, jnp.zeros_like(readout))
        return out

    def _L0_ffn_ref(x, Wr, Wg, Wu, Wd):
        import jax, jax.numpy as jnp
        import numpy as np
        B, T, D = (4, 256, 256)
        E = 8
        K = 2
        F = 1024 // (E // 2)
        probs = jax.nn.softmax(x @ Wr, axis=-1)
        topk_w, topk_idx = jax.lax.top_k(probs, K)
        topk_w = topk_w / jnp.sum(topk_w, axis=-1, keepdims=True)
        output = jnp.zeros_like(x)
        for i in range(E):
            sel = topk_idx == i
            w_i = jnp.sum(topk_w * sel.astype(x.dtype), axis=-1, keepdims=True)
            h = jax.nn.silu(x @ Wg[i]) * (x @ Wu[i])
            e_out = h @ Wd[i]
            output = output + w_i * e_out
        return output

    def _L1_xattn_ref(x, W_qkv, W_o, beta_q, beta_k, gate, log_tau, K_mem, V_mem, clip_k):
        import jax, jax.numpy as jnp
        import numpy as np
        D = x.shape[-1]
        scale = D ** (-0.5)
        qkv = x @ W_qkv.T
        Q = qkv[..., :D]
        alpha = jax.nn.sigmoid(gate)
        tau = jnp.exp(log_tau)
        coef = (alpha * beta_q + (1.0 - alpha) * beta_k) * scale * tau
        scores = coef * jnp.einsum('bsd,bnd->bsn', Q, K_mem)
        scores = scores - jnp.max(scores, axis=-1, keepdims=True)
        thr = jax.lax.top_k(scores, clip_k)[0][..., -1:]
        scores = jnp.where(scores < thr, -jnp.inf, scores)
        att = jax.nn.softmax(scores, axis=-1)
        out = jnp.einsum('bsn,bnd->bsd', att, V_mem)
        return out @ W_o.T

    def _L1_ffn_ref(x, w1, w2):
        import jax, jax.numpy as jnp
        import numpy as np
        EPS = 1e-05

        def activation_quant(x):
            scale = 127.0 / jnp.clip(jnp.max(jnp.abs(x), axis=-1, keepdims=True), EPS, None)
            return jnp.clip(jnp.round(x * scale), -128.0, 127.0) / scale

        def weight_quant(w):
            scale = 1.0 / jnp.clip(jnp.mean(jnp.abs(w)), EPS, None)
            return jnp.clip(jnp.round(w * scale), -1.0, 1.0) / scale

        def bitlinear(x, w):
            xq = x + jax.lax.stop_gradient(activation_quant(x) - x)
            wq = w + jax.lax.stop_gradient(weight_quant(w) - w)
            return jnp.einsum('bsd,hd->bsh', xq, wq)
        h = bitlinear(x, w1)
        h = jax.nn.gelu(h, approximate=False)
        return bitlinear(h, w2)
    x = x + _L0_xattn_ref(_layernorm(x, axis=-1), ctx_2048, mask_BxS2_bk0)
    x = x + _L0_ffn_ref(_layernorm(x, axis=-1), L0_ffn_Wr, L0_ffn_Wg, L0_ffn_Wu, L0_ffn_Wd)
    x = x + _L1_xattn_ref(_layernorm(x, axis=-1), L1_xattn_W_qkv, L1_xattn_W_o, L1_xattn_beta_q, L1_xattn_beta_k, L1_xattn_gate, L1_xattn_log_tau, ctx_2048, ctx_2048, 54)
    x = x + _L1_ffn_ref(_layernorm(x, axis=-1), L1_ffn_w1, L1_ffn_w2)
    return x

_drawn_inputs = setup_inputs


def setup_inputs(seed=0):
    import zlib

    import numpy as np

    out = dict(_drawn_inputs(seed))
    spreads = {}
    factors = {}
    for name, (base, spread) in spreads.items():
        noise = np.random.default_rng([zlib.crc32(name.encode()), seed]).standard_normal(out[name].shape)
        drawn = base * np.exp(spread * noise) if base else spread * noise
        out[name] = jnp.asarray(drawn.astype(out[name].dtype))
    for name, factor in factors.items():
        out[name] = (out[name] * factor).astype(out[name].dtype)
    return out
```

```python
from contextlib import ExitStack

import numpy as np

import concourse.bass as bass
from concourse import mybir

F32 = mybir.dt.float32
F32R = mybir.dt.float32r
BF16 = mybir.dt.bfloat16
U8 = mybir.dt.uint8
U32 = mybir.dt.uint32
ALU = mybir.AluOpType
ACT = mybir.ActivationFunctionType
AX = mybir.AxisListType

P = 128
B, S, D = 4, 256, 256
M = 1601
E = 8
F = 256
H4 = 1024
TOPK = 54
KC = D // P
NT = B * S // P
TB = S // P
EPS = 1e-5
SCALE = float(D) ** -0.5
NEG = -1.6e31
BELOW_ALL = -3.0e38
MAGIC = 12582912.0

MW = M + M % 2
KCHUNKS = [(c, min(512, MW - c)) for c in range(0, MW, 512)]
NKC = len(KCHUNKS)
NMC = -(-M // P)
MROWS = [min(P, M - P * m) for m in range(NMC)]
NU = -(-NMC // 2)
UNITS = [[m for m in (2 * u, 2 * u + 1) if m < NMC] for u in range(NU)]
NVP = -(-NMC // 4)

RING = 6
LOOK = RING - 2
STAGE = 3
NPT = 2
NHT = 3
NQA = 2
NXT = 4


def half_steps(h):
    b0, b1 = 2 * h, 2 * h + 1
    q = 6 * h
    s = []
    s += [("mask", b0), ("ln", q, b0), ("xT", q), ("scores1", b0), ("ln", q + 1, b1), ("xT", q + 1)]
    if h == 0:
        s += [("mask", b1), ("scores1", b1), ("pv1", b0), ("pv1", b1), ("wload", 1)]
    else:
        s += [("pv1", b0), ("mask", b1), ("scores1", b1), ("pv1", b1)]
    s += [("ln", q + 2, b0), ("xT", q + 2), ("ln", q + 3, b1), ("xT", q + 3), ("router", h)]
    for e in range(E):
        s.append(("gu", h, e, 0))
        if e:
            s.append(("down", h, e - 1))
        s.append(("gu", h, e, 1))
        if h == 0 and e == 0:
            s += [("coef",), ("wquant", 1), ("wload", 2), ("wquant", 2)]
        if h == 1 and e == 1:
            s += [("exp3", 0), ("exp3", 1), ("pv3", 0), ("wo", 0)]
            s += quant_steps(0)
        if h == 1 and e == 5:
            s += [("exp3", 2), ("exp3", 3), ("pv3", 1), ("wo", 1)]
            s += quant_steps(1)
    s += [("down", h, E - 1)]
    s += [("ln", q + 4, b0), ("xT", q + 4), ("ln", q + 5, b1), ("xT", q + 5)]
    s += [("qT", b0), ("scores3", b0), ("qT", b1), ("scores3", b1)]
    if h == 1:
        for b in (b0, b1):
            s += [("exp3", 2 * b), ("exp3", 2 * b + 1), ("pv3", b), ("wo", b)] + quant_steps(b)
    return s


def quant_steps(b):
    s = [("ln4", b), ("q4", b)]
    for t in (2 * b, 2 * b + 1):
        s += [("up4", t), ("h4T", t), ("down4", t)]
    return s


STEPS = half_steps(0) + half_steps(1)


def number(wanted):
    found = {}
    for step in STEPS:
        for key in wanted(step):
            found[key] = len(found)
    return found


T_UNIT = number(lambda s: {
    "xT": lambda: [s], "q4": lambda: [s], "h4T": lambda: [s],
    "pv1": lambda: [("p1", s[1], u) for u in range(NU)],
    "pv3": lambda: [("p3", s[1], u) for u in range(NU)]}.get(s[0], lambda: [])())
T_SPLIT = {k: i for i, k in enumerate(k for k in T_UNIT if k[0] in ("xT", "p1", "p3"))}
P_UNIT = {k: i for i, k in enumerate(k for k in T_UNIT if k[0] in ("p1", "p3"))}
S_UNIT = number(lambda s: {
    "scores1": lambda: [("s1", 2 * s[1] + i, c) for c in range(NKC) for i in range(TB)],
    "scores3": lambda: [("s3", 2 * s[1] + i, c) for c in range(NKC) for i in range(TB)],
    "up4": lambda: [("up4", s[1], n) for n in range(2)]}.get(s[0], lambda: [])())
S3_UNIT = {k: i for i, k in enumerate(k for k in S_UNIT if k[0] == "s3")}
O_UNIT = number(lambda s: {
    "pv1": lambda: [("pv1", 2 * s[1] + i) for i in range(TB)],
    "router": lambda: [s], "coef": lambda: [],
    "down": lambda: [(*s, i) for i in range(4)],
    "qT": lambda: [s],
    "pv3": lambda: [("aT", s[1], d) for d in range(KC)],
    "wo": lambda: [("wo", 2 * s[1] + i) for i in range(TB)],
    "wquant": lambda: [s],
    "down4": lambda: [s]}.get(s[0], lambda: [])())
O_SPLIT = {k: i for i, k in enumerate(k for k in O_UNIT if k[0] in ("qT", "aT"))}
PIECE = number(lambda s: {
    "scores1": lambda: [("k1", s[1], c) for c in range(NKC)],
    "scores3": lambda: [("k3", s[1], c) for c in range(NKC)],
    "pv1": lambda: [("v1", s[1], g) for g in range(NVP)],
    "pv3": lambda: [("v3", s[1], g) for g in range(NVP)],
    "gu": lambda: [("gu", s[1], s[2])] if s[3] == 1 else [],
    "down": lambda: [("wd", s[1], s[2])]}.get(s[0], lambda: [])())
PIECES = list(PIECE)
QA_USE = number(lambda s: [s] if s[0] == "qT" else [("aT", s[1])] if s[0] == "pv3" else [])
XT_USE = number(lambda s: [s[1]] if s[0] == "xT" else [])
LN_USE = number(lambda s: [s] if s[0] in ("ln", "ln4") else [])

S1_BUF = {0: 4, 1: 5, 2: 0, 3: 1, 4: 4, 5: 5, 6: 4, 7: 5}
S3_BUF = {t: t % 4 for t in range(NT)}
E3_BUF = {t: 6 + t % 2 for t in range(NT)}


def two_layers(nc, x, ctx, ctxT, mask, Wr, Wg, Wu, Wd, WqT, WoT, beta_q, beta_k, gate, log_tau, w1T, w2T, out):
    es = ExitStack()
    with es:
        def sb(name, shape, dt=F32):
            return es.enter_context(nc.sbuf_tensor(name, shape, dt))

        def sem(name):
            return es.enter_context(nc.semaphore(name))

        stage = sb("stage", [P, STAGE, 1024])
        ring_hi = sb("ring_hi", [P, RING, 1024], F32R)
        ring_lo = sb("ring_lo", [P, RING, 1024], F32R)
        rows = sb("rows", [P, 8, MW])
        x_res = sb("x_res", [P, NT, D])
        xn = sb("xn", [P, TB, D])
        xT_hi = sb("xT_hi", [P, NXT, KC, S], F32R)
        xT_lo = sb("xT_lo", [P, NXT, KC, S], F32R)
        pT_hi = sb("pT_hi", [P, NPT, 2, TB, P], F32R)
        pT_lo = sb("pT_lo", [P, NPT, 2, TB, P], F32R)
        qa_hi = sb("qa_hi", [P, NQA, KC, S], F32R)
        qa_lo = sb("qa_lo", [P, NQA, KC, S], F32R)
        hid = sb("hid", [P, 2, 512])
        hT_hi = sb("hT_hi", [P, NHT, 512], F32R)
        hT_lo = sb("hT_lo", [P, NHT, 512], F32R)
        fixed_hi = sb("fixed_hi", [P, 2, KC, D], F32R)
        fixed_lo = sb("fixed_lo", [P, 2, KC, D], F32R)
        wr_raw = sb("wr_raw", [P, KC, E])
        wr_hi = sb("wr_hi", [P, KC, E], F32R)
        wr_lo = sb("wr_lo", [P, KC, E], F32R)
        w1q = sb("w1q", [P, KC, H4], BF16)
        w2q = sb("w2q", [P, H4 // P, D], BF16)
        mask_u8 = sb("mask_u8", [P, M], U8)
        mask_add = sb("mask_add", [P, MW], BF16)
        cand = sb("cand", [P, 8])
        gel = sb("gel", [P, H4])
        gel_q = sb("gel_q", [P, H4], BF16)
        gelT = sb("gelT", [P, H4], BF16)
        xq = sb("xq", [P, TB, D], BF16)
        xqT = sb("xqT", [P, KC, TB, P], BF16)
        fin = sb("fin", [P, D])
        ident = sb("ident", [P, P])
        ident_b = sb("ident_b", [P, P], BF16)
        ones = sb("ones", [P, P])
        iota8 = sb("iota8", [P, E])
        minus_half = sb("minus_half", [P, TB])
        bn = sb("bn", [P, TB, 6])
        mv = sb("mv", [P, TB, 2])
        var_eps = sb("var_eps", [P, TB])
        rstd = sb("rstd", [P, TB])
        mx1c = sb("mx1c", [P, TB, NKC])
        mx1 = sb("mx1", [P, NT])
        nm1 = sb("nm1", [P, NT])
        sum1 = sb("sum1", [P, NT])
        r1 = sb("r1", [P, NT])
        top8 = sb("top8", [P, 4, 8])
        idx8 = sb("idx8", [P, 4, 8], U32)
        idxf = sb("idxf", [P, 4, 8])
        logits = sb("logits", [P, 4, E])
        gap = sb("gap", [P, 4])
        egap = sb("egap", [P, 4])
        w_top = sb("w_top", [P, 2, 4])
        w_tmp = sb("w_tmp", [P, 4, E])
        w_sel = sb("w_sel", [P, 4, E])
        nmax3 = sb("nmax3", [P, NT])
        thr3 = sb("thr3", [P, NT])
        sum3 = sb("sum3", [P, NT])
        r3 = sb("r3", [P, NT])
        scal = sb("scal", [P, 12])
        wabs = sb("wabs", [P, 2])
        wsum = sb("wsum", [P, 2])
        wdeq = sb("wdeq", [P, 2])
        wscl = sb("wscl", [P, 2])
        xmx = sb("xmx", [P, TB])
        xinv = sb("xinv", [P, TB])
        xscl = sb("xscl", [P, TB])
        xdeq = sb("xdeq", [P, TB])
        gmx = sb("gmx", [P, 1])
        ginv = sb("ginv", [P, 1])
        gscl = sb("gscl", [P, 1])
        gdeq = sb("gdeq", [P, 1])

        def bank(name):
            return es.enter_context(nc.psum_tensor(name, [P, 512], F32))

        S_bank = [bank("S0"), bank("S1")]
        T_bank = [bank("T0"), bank("T1")]
        O_bank = [bank("O0"), bank("O1")]
        G_bank, U_bank = bank("G"), bank("U")

        piece_in = [sem(f"piece_in{i}") for i in range(STAGE)]
        piece_hi = sem("piece_hi")
        piece_split = sem("piece_split")
        x_in = [sem(f"x_in{b}") for b in range(B)]
        fixed_in = sem("fixed_in")
        small_in = sem("small_in")
        mask_in = sem("mask_in")
        wq_in = sem("wq_in")
        consts = sem("consts")
        wr_split = sem("wr_split")
        t_ready = sem("t_ready")
        t_hi = sem("t_hi")
        t_out = sem("t_out")
        s_ready = sem("s_ready")
        s_free = [sem("s_free0"), sem("s_free1")]
        o_ready = sem("o_ready")
        o_hi = sem("o_hi")
        o_out = sem("o_out")
        g_ready, u_ready = sem("g_ready"), sem("u_ready")
        silu_done = sem("silu_done")
        hid_done = sem("hid_done")
        hid_hi, hid_lo = sem("hid_hi"), sem("hid_lo")
        pT_used = sem("pT_used")
        var_ready, rstd_ready, xn_ready = sem("var_ready"), sem("rstd_ready"), sem("xn_ready")
        mask_ready = sem("mask_ready")
        max1_ready, exp1_done = sem("max1_ready"), sem("exp1_done")
        gap_ready, egap_ready = sem("gap_ready"), sem("egap_ready")
        s3_in = sem("s3_in")
        thr_ready = sem("thr_ready")
        exp3_done = sem("exp3_done")
        p3_ready = sem("p3_ready")
        coef_e, coef_ready = sem("coef_e"), sem("coef_ready")
        wabs_ready, w_done = sem("wabs_ready"), sem("w_done")
        xq_ready, gelu_done, gelq_ready = sem("xq_ready"), sem("gelu_done"), sem("gelq_ready")
        fin_ready = sem("fin_ready")
        stored = sem("stored")
        dve_chain = sem("dve_chain")
        pool_chain = sem("pool_chain")

        block = es.enter_context(nc.Block())

        mask = mask.bitcast(U8).rearrange("(b m) -> b m", b=B)

        def wait(eng, s, value):
            if value > 0:
                eng.wait_ge(s, value)

        def product_done(eng, key):
            if key in S_UNIT:
                eng.wait_ge(s_ready, S_UNIT[key] + 1)
            else:
                eng.wait_ge(o_ready, O_UNIT[key] + 1)

        def probabilities_done(eng, key):
            s, b, u = key
            if u == NU - 1:
                product_done(eng, ("pv1", 2 * b + 1) if s == "p1" else ("aT", b, KC - 1))
            else:
                eng.wait_ge(pT_used, P_UNIT[key] - (list(P_UNIT).index(key) - u) // NU + 1)

        def piece_done(eng, n):
            if n < 0:
                return
            kind, a, c = PIECES[n]
            if kind in ("k1", "k3"):
                product_done(eng, ("s" + kind[1], 2 * a + TB - 1, c))
            elif kind in ("v1", "v3"):
                probabilities_done(eng, ("p" + kind[1], a, min(2 * c + 1, NU - 1)))
            elif kind == "gu":
                eng.wait_ge(u_ready, 2 * (E * a + c) + 2)
            else:
                product_done(eng, ("down", a, c, 3))

        def tokens_done(eng, q):
            if q < 0:
                return
            h, stage_ = q // 6, q % 6 // 2
            if stage_ == 0:
                product_done(eng, ("s1", 4 * h + 2 * (q % 2) + 1, NKC - 1))
            elif stage_ == 1:
                eng.wait_ge(u_ready, 2 * E * (h + 1))
            else:
                product_done(eng, ("qT", 2 * h + q % 2))

        def queries_done(eng, use):
            if use < 0:
                return
            kind, b = list(QA_USE)[use]
            product_done(eng, ("s3", 2 * b + 1, NKC - 1) if kind == "qT" else ("wo", 2 * b + 1))

        def piece_shape(key):
            if key[0] in ("k1", "k3"):
                return KC, KCHUNKS[key[2]][1], P
            if key[0] in ("v1", "v3"):
                mcs = [m for m in range(4 * key[2], 4 * key[2] + 4) if m < NMC]
                return len(mcs), D, min(MROWS[m] for m in mcs)
            if key[0] == "gu":
                return 2 * KC, F, P
            return KC, D, P

        def view(buf, key):
            a, w, r = piece_shape(key)
            return buf[0:r, 0:a * w].rearrange("p (a w) -> p a w", a=a)

        def ring(key):
            n = PIECE[key] % RING
            return view(ring_hi[:, n, :], key), view(ring_lo[:, n, :], key)

        def s_bank(key):
            return S_bank[S_UNIT[key] % 2]

        def t_bank(key):
            return T_bank[T_UNIT[key] % 2]

        def o_bank(key):
            return O_bank[O_UNIT[key] % 2]

        w_raw = rows[:, 2:4, :].rearrange("p a m -> p (a m)")[:, 0:2 * H4]
        w_views = {1: (w1T.rearrange("(k p) h -> p k h", p=P), w1q), 2: (w2T.rearrange("(k p) d -> p k d", p=P), w2q)}

        @block.sync
        def _(sp):
            x_v = x.rearrange("(t p) d -> p t d", p=P)
            sp.dma_start(x_res[:, 0:2, :], x_v[:, 0:2, :]).then_inc(x_in[0], 16)
            for n, key in enumerate(PIECES):
                slot = n % STAGE
                wait(sp, piece_split, n - STAGE + 1)
                dst = view(stage[:, slot, :], key)
                kind, a = key[0], key[1]
                if kind in ("k1", "k3"):
                    c0, w = KCHUNKS[key[2]]
                    w = min(w, M - c0)
                    sp.dma_start(dst[:, :, 0:w], ctxT[a, :, c0:c0 + w].rearrange("(k p) m -> p k m", p=P)) \
                      .then_inc(piece_in[slot], 16)
                elif kind in ("v1", "v3"):
                    k, _, r = piece_shape(key)
                    m0 = 4 * P * key[2]
                    sp.dma_start(dst, ctx[a, m0:m0 + k * r, :].rearrange("(k p) d -> p k d", p=r)) \
                      .then_inc(piece_in[slot], 16)
                elif kind == "gu":
                    e = key[2]
                    sp.dma_start(dst[:, 0:KC, :], Wg[e].rearrange("(k p) f -> p k f", p=P)).then_inc(piece_in[slot], 8 * 2)
                    sp.dma_start(dst[:, KC:, :], Wu[e].rearrange("(k p) f -> p k f", p=P)).then_inc(piece_in[slot], 8 * 2)
                else:
                    sp.dma_start(dst, Wd[key[2]].rearrange("(k p) d -> p k d", p=P)).then_inc(piece_in[slot], 16)
                if n == 2:
                    for b in range(1, B):
                        sp.dma_start(x_res[:, 2 * b:2 * b + 2, :], x_v[:, 2 * b:2 * b + 2, :]).then_inc(x_in[b], 16)

        arrived, so_far = [], [0] * STAGE
        for n, key in enumerate(PIECES):
            so_far[n % STAGE] += 32 if key[0] == "gu" else 16
            arrived.append(so_far[n % STAGE])

        def hook(key, split):
            n = PIECE[key] + LOOK
            if n < len(PIECES):
                split(n)

        @block.gpsimd
        def _(pool):
            pool.memset(ident[:, :], 0.0).then_inc(pool_chain, 1)
            pool.memset(ones[:, :], 1.0).then_inc(consts, 1)
            pool.memset(minus_half[:, :], -0.5).then_inc(consts, 1)
            pool.wait_ge(pool_chain, 1)
            pool.affine_select(out=ident[:, :], in_=ident[:, :], compare_op=ALU.not_equal, fill=1.0, base=0,
                               pattern=[[-1, P]], channel_multiplier=1).then_inc(consts, 1)
            pool.memset(ident_b[:, :], 0.0).then_inc(pool_chain, 1)
            pool.wait_ge(pool_chain, 2)
            pool.affine_select(out=ident_b[:, :], in_=ident_b[:, :], compare_op=ALU.not_equal, fill=1.0, base=0,
                               pattern=[[-1, P]], channel_multiplier=1).then_inc(consts, 1)
            for e in range(E):
                pool.memset(iota8[:, e:e + 1], float(e)).then_inc(consts, 1)
            pool.wait_ge(consts, 4 + E)

            def split_lo(n):
                key = PIECES[n]
                pool.wait_ge(piece_hi, n + 1)
                hi, lo = ring(key)
                pool.tensor_tensor(lo, view(stage[:, n % STAGE, :], key), hi.bitcast(F32), ALU.subtract) \
                    .then_inc(piece_split, 1)

            for n in range(LOOK):
                split_lo(n)
            hidden = 0
            for step in STEPS:
                kind = step[0]
                if kind in ("ln", "ln4"):
                    n = LN_USE[step]
                    pool.wait_ge(var_ready, n + 1)
                    pool.tensor_tensor(rstd[:, :], var_eps[:, :], minus_half[:, :], ALU.pow).then_inc(rstd_ready, 1)
                elif kind in ("scores1", "scores3"):
                    for c in range(NKC):
                        hook(("k" + kind[-1], step[1], c), split_lo)
                elif kind in ("pv1", "pv3"):
                    for g in range(NVP):
                        hook(("v" + kind[-1], step[1], g), split_lo)
                elif kind == "down":
                    hook(("wd", step[1], step[2]), split_lo)
                elif kind == "gu":
                    if step[3] == 1:
                        hook(("gu", step[1], step[2]), split_lo)
                    j = hidden
                    hidden += 1
                    pool.wait_ge(hid_hi, j + 1)
                    pool.tensor_tensor(hT_lo[:, j % NHT, :], hid[:, j % 2, :], hT_hi[:, j % NHT, :].bitcast(F32),
                                       ALU.subtract).then_inc(hid_lo, 1)

        @block.scalar
        def _(act):
            for i, (w_name, w) in enumerate((("q", WqT), ("o", WoT))):
                act.dma_start(rows[:, 6 + i, 0:KC * D].rearrange("p (k d) -> p k d", k=KC),
                              w.rearrange("(k p) d -> p k d", p=P)).then_inc(fixed_in, 16)
            act.dma_start(wr_raw[:, :, :], Wr.rearrange("(k p) e -> p k e", p=P)).then_inc(fixed_in, 16)
            for i, s in enumerate((beta_q, beta_k, gate, log_tau)):
                act.dma_start(scal[:, i:i + 1], s.partition_broadcast(P)).then_inc(small_in, 16)

            def split_hi(n):
                key = PIECES[n]
                act.wait_ge(piece_in[n % STAGE], arrived[n])
                piece_done(act, n - RING)
                act.activation(ring(key)[0], view(stage[:, n % STAGE, :], key), ACT.Copy).then_inc(piece_hi, 1)

            act.wait_ge(consts, 4 + E)
            for n in range(LOOK):
                split_hi(n)

            def t_hi_out(key, dst, src):
                act.wait_ge(t_ready, T_UNIT[key] + 1)
                act.activation(dst, src, ACT.Copy).then_inc(t_hi, 1)

            hidden = 0
            for step in STEPS:
                kind = step[0]
                if kind == "mask":
                    b = step[1]
                    if b:
                        act.wait_ge(mask_ready, b)
                        act.wait_ge(max1_ready, 2 * b)
                    act.dma_start(mask_u8[:, :], mask[b:b + 1, :].partition_broadcast(P)).then_inc(mask_in, 16)
                    act.wait_ge(mask_in, 16 * (b + 1))
                    act.activation(mask_add[:, 0:M], mask_u8[:, :], ACT.Copy, scale=-NEG, bias=NEG).then_inc(mask_ready, 1)
                elif kind == "xT":
                    q = step[1]
                    tokens_done(act, q - NXT)
                    t_hi_out(step, xT_hi[:, q % NXT, :, :].rearrange("p k s -> p (k s)"), t_bank(step)[:, :])
                elif kind == "scores1":
                    b = step[1]
                    for c in range(NKC):
                        hook(("k1", b, c), split_hi)
                    for t in (2 * b, 2 * b + 1):
                        act.wait_ge(max1_ready, t + 1)
                        row = rows[:, S1_BUF[t], 0:M]
                        act.activation(row, row, ACT.Exp, bias=nm1[:, t:t + 1], scale=SCALE,
                                       accum_out=sum1[:, t:t + 1]).then_inc(exp1_done, 1)
                elif kind in ("pv1", "pv3"):
                    b, s = step[1], kind[-1]
                    for u, mcs in enumerate(UNITS):
                        if u % 2 == 0:
                            hook(("v" + s, b, u // 2), split_hi)
                        key = ("p" + s, b, u)
                        pu = P_UNIT[key]
                        r, w = MROWS[mcs[-1]], len(mcs) * TB * P
                        if pu >= NPT:
                            probabilities_done(act, list(P_UNIT)[pu - NPT])
                        t_hi_out(key, pT_hi[0:r, pu % NPT, :, :, :].rearrange("p a i s -> p (a i s)")[:, 0:w],
                                 t_bank(key)[0:r, 0:w])
                    if kind == "pv3":
                        use = QA_USE[("aT", b)]
                        queries_done(act, use - NQA)
                        for d in range(KC):
                            key = ("aT", b, d)
                            act.wait_ge(o_ready, O_UNIT[key] + 1)
                            act.activation(qa_hi[:, use % NQA, d, :], o_bank(key)[:, 0:S], ACT.Copy).then_inc(o_hi, 1)
                elif kind == "router":
                    act.wait_ge(gap_ready, step[1] + 1)
                    act.activation(egap[:, :], gap[:, :], ACT.Exp).then_inc(egap_ready, 1)
                elif kind == "gu":
                    if step[3] == 1:
                        hook(("gu", step[1], step[2]), split_hi)
                    j = hidden
                    hidden += 1
                    act.wait_ge(g_ready, j + 1)
                    wait(act, hid_lo, j - 1)
                    act.activation(hid[:, j % 2, :], G_bank[:, :], ACT.Silu).then_inc(silu_done, 1)
                    act.wait_ge(hid_done, j + 1)
                    if j >= NHT:
                        product_done(act, ("down", (j - NHT) // 2 // E, (j - NHT) // 2 % E, 3))
                    act.activation(hT_hi[:, j % NHT, :], hid[:, j % 2, :], ACT.Copy).then_inc(hid_hi, 1)
                elif kind == "down":
                    hook(("wd", step[1], step[2]), split_hi)
                elif kind == "coef":
                    act.wait_ge(small_in, 64)
                    act.activation(scal[:, 4:5], scal[:, 2:3], ACT.Exp, scale=-1.0).then_inc(coef_e, 1)
                    act.activation(scal[:, 5:6], scal[:, 3:4], ACT.Exp).then_inc(coef_e, 1)
                elif kind == "wload":
                    which = step[1]
                    if which == 1:
                        act.wait_ge(fixed_in, 48)
                    else:
                        act.wait_ge(w_done, 1)
                    v = w_views[which][0]
                    act.dma_start(w_raw.rearrange("p (k n) -> p k n", k=v.shape[1]), v).then_inc(wq_in, 16)
                elif kind == "qT":
                    b = step[1]
                    use = QA_USE[step]
                    act.wait_ge(coef_ready, 1)
                    queries_done(act, use - NQA)
                    act.wait_ge(o_ready, O_UNIT[step] + 1)
                    act.activation(qa_hi[:, use % NQA, :, :].rearrange("p k s -> p (k s)"), o_bank(step)[:, :],
                                   ACT.Copy, scale=scal[:, 11:12]).then_inc(o_hi, 1)
                elif kind == "scores3":
                    b = step[1]
                    for c, (c0, w) in enumerate(KCHUNKS):
                        hook(("k3", b, c), split_hi)
                        w = min(w, M - c0)
                        for i in range(TB):
                            t = 2 * b + i
                            key = ("s3", t, c)
                            if c == 0:
                                if t < 4:
                                    act.wait_ge(t_ready, T_UNIT[("p1", 1, NU - 1)] + 1)
                                    act.wait_ge(w_done, 2)
                                else:
                                    act.wait_ge(p3_ready, t - 3)
                            act.wait_ge(s_ready, S_UNIT[key] + 1)
                            act.activation(rows[:, S3_BUF[t], c0:c0 + w], s_bank(key)[:, 0:w], ACT.Copy) \
                               .then_inc(s3_in, 1)
                elif kind == "exp3":
                    t = step[1]
                    act.wait_ge(thr_ready, t + 1)
                    if t >= 2:
                        act.wait_ge(t_ready, T_UNIT[("p3", t // 2 - 1, NU - 1)] + 1)
                    act.activation(rows[:, E3_BUF[t], 0:M], rows[:, S3_BUF[t], 0:M], ACT.Exp,
                                   bias=nmax3[:, t:t + 1]).then_inc(exp3_done, 1)
                elif kind == "up4":
                    t = step[1]
                    for n in range(2):
                        key = ("up4", t, n)
                        if n == 0:
                            wait(act, gelq_ready, t)
                        act.wait_ge(s_ready, S_UNIT[key] + 1)
                        act.activation(gel[:, 512 * n:512 * n + 512], s_bank(key)[:, :], ACT.Gelu,
                                       scale=xdeq[:, t % 2:t % 2 + 1]).then_inc(gelu_done, 1)
                elif kind == "down4":
                    t = step[1]
                    act.wait_ge(fin_ready, t + 1)
                    act.dma_start(out[P * t:P * t + P, :], fin[:, :]).then_inc(stored, 16)
            act.wait_ge(stored, 16 * NT)

        @block.tensor
        def _(pe):
            def product(dst, a, b, first, last):
                pe.matmul(dst, a[0], b[0], start=first, stop=False)
                pe.matmul(dst, a[0], b[1], start=False, stop=False)
                return pe.matmul(dst, a[1], b[0], start=False, stop=last)

            def t_free(key):
                wait(pe, t_out, T_UNIT[key] - 1)

            def o_free(key):
                wait(pe, o_out, O_UNIT[key] - 1)

            def s_bank_free(key):
                n = S_UNIT[key]
                prev = [k for k, v in S_UNIT.items() if v == n - 2]
                if not prev:
                    return
                k = prev[0]
                if k[0] == "s1":
                    pe.wait_ge(s_free[n % 2], s1_count[n % 2][k])
                elif k[0] == "s3":
                    pe.wait_ge(s3_in, S3_UNIT[k] + 1)
                else:
                    pe.wait_ge(gelu_done, 2 * k[1] + k[2] + 1)

            s1_count = [{}, {}]
            for k, v in S_UNIT.items():
                if k[0] == "s1":
                    s1_count[v % 2][k] = len(s1_count[v % 2]) + 1

            def xT(q, k):
                return xT_hi[:, q % NXT, k, :], xT_lo[:, q % NXT, k, :]

            def transpose_probabilities(b, u, s):
                key = ("p" + s, b, u)
                mcs = UNITS[u]
                t_free(key)
                for i in range(TB):
                    t = 2 * b + i
                    if u == 0:
                        if s == "1":
                            pe.wait_ge(exp1_done, t + 1)
                        else:
                            pe.wait_ge(p3_ready, t + 1)
                    buf = (S1_BUF if s == "1" else E3_BUF)[t]
                    for a, m in enumerate(mcs):
                        r = MROWS[m]
                        mm = pe.transpose(t_bank(key)[0:r, (2 * a + i) * P:(2 * a + i + 1) * P],
                                          rows[:, buf, m * P:m * P + r], ident[:, :])
                mm.then_inc(t_ready, 1)

            pe.wait_ge(consts, 4 + E)
            hidden = 0
            for step in STEPS:
                kind = step[0]
                if kind == "xT":
                    q = step[1]
                    t_free(step)
                    pe.wait_ge(xn_ready, q + 1)
                    for k in range(KC):
                        for i in range(TB):
                            mm = pe.transpose(t_bank(step)[:, (2 * k + i) * P:(2 * k + i + 1) * P],
                                              xn[:, i, k * P:(k + 1) * P], ident[:, :])
                    mm.then_inc(t_ready, 1)
                elif kind in ("scores1", "scores3"):
                    b, s = step[1], kind[-1]
                    if s == "1":
                        q = 6 * (b // 2) + b % 2
                        pe.wait_ge(t_out, T_UNIT[("xT", q)] + 1)
                        lhs_hi, lhs_lo = xT_hi[:, q % NXT], xT_lo[:, q % NXT]
                    else:
                        use = QA_USE[("qT", b)]
                        pe.wait_ge(o_out, O_UNIT[("qT", b)] + 1)
                        lhs_hi, lhs_lo = qa_hi[:, use % NQA], qa_lo[:, use % NQA]
                    for c, (c0, w) in enumerate(KCHUNKS):
                        piece = ("k" + s, b, c)
                        pe.wait_ge(piece_split, PIECE[piece] + 1)
                        hi, lo = ring(piece)
                        for i in range(TB):
                            key = ("s" + s, 2 * b + i, c)
                            s_bank_free(key)
                            for k in range(KC):
                                mm = product(s_bank(key)[:, 0:w],
                                             (lhs_hi[:, k, i * P:(i + 1) * P], lhs_lo[:, k, i * P:(i + 1) * P]),
                                             (hi[:, k, :], lo[:, k, :]), k == 0, k == KC - 1)
                            mm.then_inc(s_ready, 1)
                elif kind in ("pv1", "pv3"):
                    b, s = step[1], kind[-1]
                    transpose_probabilities(b, 0, s)
                    transpose_probabilities(b, 1, s)
                    for u, mcs in enumerate(UNITS):
                        key = ("p" + s, b, u)
                        slot = P_UNIT[key] % NPT
                        piece = ("v" + s, b, u // 2)
                        pe.wait_ge(t_out, T_UNIT[key] + 1)
                        if u % 2 == 0:
                            pe.wait_ge(piece_split, PIECE[piece] + 1)
                        hi, lo = ring(piece)
                        for o in range(2):
                            dst_key = ("pv1", 2 * b + o) if s == "1" else ("aT", b, o)
                            if u == 0:
                                o_free(dst_key)
                            for a, m in enumerate(mcs):
                                r, v = MROWS[m], m % 4
                                first, last = m == 0, m == NMC - 1
                                if s == "1":
                                    mm = product(o_bank(dst_key)[:, 0:D],
                                                 (pT_hi[0:r, slot, a, o, :], pT_lo[0:r, slot, a, o, :]),
                                                 (hi[0:r, v, :], lo[0:r, v, :]), first, last)
                                else:
                                    mm = product(o_bank(dst_key)[:, 0:S],
                                                 (hi[0:r, v, o * P:(o + 1) * P], lo[0:r, v, o * P:(o + 1) * P]),
                                                 (pT_hi[0:r, slot, a, :, :], pT_lo[0:r, slot, a, :, :]), first, last)
                            if u == NU - 1:
                                mm.then_inc(o_ready, 1)
                        if u < NU - 1:
                            mm.then_inc(pT_used, 1)
                        if u + 2 < NU:
                            transpose_probabilities(b, u + 2, s)
                elif kind == "router":
                    h = step[1]
                    q = 6 * h + 2
                    pe.wait_ge(t_out, T_UNIT[("xT", q + 1)] + 1)
                    pe.wait_ge(wr_split, 2)
                    o_free(step)
                    for i in range(4):
                        for k in range(KC):
                            hi, lo = xT(q + i // 2, k)
                            cols = slice((i % 2) * P, (i % 2 + 1) * P)
                            mm = product(o_bank(step)[:, i * E:(i + 1) * E], (hi[:, cols], lo[:, cols]),
                                         (wr_hi[:, k, :], wr_lo[:, k, :]), k == 0, k == KC - 1)
                    mm.then_inc(o_ready, 1)
                elif kind == "gu":
                    _, h, e, f = step
                    q = (6 * h + 2) % NXT
                    j = hidden
                    hidden += 1
                    piece = ("gu", h, e)
                    pe.wait_ge(piece_split, PIECE[piece] + 1)
                    hi, lo = ring(piece)
                    for gate_or_up, (bank_, freed, ready) in enumerate(((G_bank, silu_done, g_ready),
                                                                        (U_bank, hid_done, u_ready))):
                        wait(pe, freed, j)
                        for k in range(KC):
                            kk = gate_or_up * KC + k
                            mm = product(bank_[:, :].rearrange("p (a s) -> p a s", a=2),
                                         (hi[:, kk, f * P:(f + 1) * P], lo[:, kk, f * P:(f + 1) * P]),
                                         (xT_hi[:, q:q + 2, k, :], xT_lo[:, q:q + 2, k, :]), k == 0, k == KC - 1)
                        mm.then_inc(ready, 1)
                elif kind == "down":
                    _, h, e = step
                    piece = ("wd", h, e)
                    pe.wait_ge(piece_split, PIECE[piece] + 1)
                    j0 = 2 * (E * h + e)
                    pe.wait_ge(hid_lo, j0 + 2)
                    hi, lo = ring(piece)
                    for i in range(4):
                        key = (*step, i)
                        o_free(key)
                        for f in range(2):
                            slot = (j0 + f) % NHT
                            mm = product(o_bank(key)[:, 0:D],
                                         (hT_hi[:, slot, i * P:(i + 1) * P], hT_lo[:, slot, i * P:(i + 1) * P]),
                                         (hi[:, f, :], lo[:, f, :]), f == 0, f == 1)
                        mm.then_inc(o_ready, 1)
                elif kind == "wquant":
                    pe.wait_ge(wabs_ready, step[1])
                    o_free(step)
                    pe.matmul(o_bank(step)[:, 0:2], ones[:, :], wabs[:, 0:2], start=True, stop=True).then_inc(o_ready, 1)
                elif kind == "qT":
                    b = step[1]
                    q = 6 * (b // 2) + 4 + b % 2
                    pe.wait_ge(t_out, T_UNIT[("xT", q)] + 1)
                    o_free(step)
                    for j in range(KC):
                        for k in range(KC):
                            mm = product(o_bank(step)[:, j * S:(j + 1) * S],
                                         (fixed_hi[:, 0, k, j * P:(j + 1) * P], fixed_lo[:, 0, k, j * P:(j + 1) * P]),
                                         xT(q, k), k == 0, k == KC - 1)
                    mm.then_inc(o_ready, 1)
                elif kind == "wo":
                    b = step[1]
                    slot = QA_USE[("aT", b)] % NQA
                    pe.wait_ge(o_out, O_UNIT[("aT", b, KC - 1)] + 1)
                    for i in range(TB):
                        key = ("wo", 2 * b + i)
                        o_free(key)
                        for k in range(KC):
                            mm = product(o_bank(key)[:, 0:D],
                                         (qa_hi[:, slot, k, i * P:(i + 1) * P], qa_lo[:, slot, k, i * P:(i + 1) * P]),
                                         (fixed_hi[:, 1, k, :], fixed_lo[:, 1, k, :]), k == 0, k == KC - 1)
                        mm.then_inc(o_ready, 1)
                elif kind == "q4":
                    b = step[1]
                    t_free(step)
                    pe.wait_ge(xq_ready, b + 1)
                    tb = t_bank(step)[:, :].bitcast(BF16)
                    for k in range(KC):
                        for i in range(TB):
                            mm = pe.transpose(tb[:, (2 * k + i) * P:(2 * k + i + 1) * P], xq[:, i, k * P:(k + 1) * P],
                                              ident_b[:, :])
                    mm.then_inc(t_ready, 1)
                elif kind == "up4":
                    t = step[1]
                    pe.wait_ge(t_out, T_UNIT[("q4", t // 2)] + 1)
                    pe.wait_ge(w_done, 2)
                    for n in range(2):
                        key = ("up4", t, n)
                        s_bank_free(key)
                        for k in range(KC):
                            mm = pe.matmul(s_bank(key)[:, :], xqT[:, k, t % 2, :], w1q[:, k, 512 * n:512 * n + 512],
                                           start=k == 0, stop=k == KC - 1)
                        mm.then_inc(s_ready, 1)
                elif kind == "h4T":
                    t = step[1]
                    t_free(step)
                    pe.wait_ge(gelq_ready, t + 1)
                    tb = t_bank(step)[:, :].bitcast(BF16)
                    for k in range(H4 // P):
                        mm = pe.transpose(tb[:, k * P:(k + 1) * P], gel_q[:, k * P:(k + 1) * P], ident_b[:, :])
                    mm.then_inc(t_ready, 1)
                elif kind == "down4":
                    t = step[1]
                    pe.wait_ge(t_out, T_UNIT[("h4T", t)] + 1)
                    o_free(step)
                    for k in range(H4 // P):
                        mm = pe.matmul(o_bank(step)[:, 0:D], gelT[:, k * P:(k + 1) * P], w2q[:, k, :],
                                       start=k == 0, stop=k == H4 // P - 1)
                    mm.then_inc(o_ready, 1)

        @block.vector
        def _(dve):
            links = [0]

            def link(ins):
                links[0] += 1
                ins.then_inc(dve_chain, 1)
                dve.wait_ge(dve_chain, links[0])

            def t_lo_out(key, dst, src, hi):
                dve.wait_ge(t_hi, T_SPLIT[key] + 1)
                dve.tensor_tensor(dst, src, hi.bitcast(F32), ALU.subtract).then_inc(t_out, 1)

            def normalise(step):
                b, n = step[-1], LN_USE[step]
                if n < 2 or step[0] == "ln" and step[1] in (6, 7):
                    dve.wait_ge(x_in[b], 16)
                else:
                    dve.wait_ge(o_out, last_update(step))
                for i in range(TB):
                    last = dve.bn_stats(bn[:, i, :], x_res[:, 2 * b + i, :])
                link(last)
                for i in range(TB):
                    last = dve.bn_aggr(mv[:, i, :], bn[:, i, :])
                link(last)
                dve.tensor_scalar(var_eps[:, :], mv[:, :, 1], EPS, None, ALU.add).then_inc(var_ready, 1)
                dve.wait_ge(rstd_ready, n + 1)
                prev = [k for k in XT_USE if T_UNIT[("xT", k)] < T_HERE[step]]
                if prev:
                    dve.wait_ge(t_ready, T_UNIT[("xT", prev[-1])] + 1)
                for i in range(TB):
                    last = dve.tensor_scalar(xn[:, i, :], x_res[:, 2 * b + i, :], mv[:, i, 0:1], rstd[:, i:i + 1],
                                             ALU.subtract, ALU.mult)
                if step[0] == "ln":
                    last.then_inc(xn_ready, 1)
                if step[0] == "ln4":
                    link(last)

            T_HERE, O_HERE, nt, no = {}, {}, 0, 0
            t_steps = {}
            for step in STEPS:
                T_HERE[step] = nt
                O_HERE[step] = no
                nt += sum(1 for k in T_UNIT if owner(k) == step)
                no += sum(1 for k in O_UNIT if owner(k) == step)

            def last_update(step):
                return O_HERE[step]

            def topk_work():
                for t in range(NT):
                    src = rows[:, S3_BUF[t], 0:M]
                    work = rows[:, E3_BUF[t], 0:M]
                    dve.wait_ge(s3_in, S3_UNIT[("s3", t, NKC - 1)] + 1)
                    if t >= 2:
                        dve.wait_ge(t_ready, T_UNIT[("p3", t // 2 - 1, NU - 1)] + 1)
                    rounds = -(-TOPK // 8)
                    for r in range(rounds):
                        link(dve.max(cand[:, :], src if r == 0 else work))
                        if r == 0:
                            dve.tensor_scalar(nmax3[:, t:t + 1], cand[:, 0:1], -1.0, None, ALU.mult)
                        yield None
                        if r < rounds - 1:
                            link(dve.match_replace(work, cand[:, :], src if r == 0 else work, BELOW_ALL))
                            yield None
                    at = (TOPK - 1) % 8
                    dve.tensor_copy(thr3[:, t:t + 1], cand[:, at:at + 1]).then_inc(thr_ready, 1)
                    yield t

            topk = topk_work()
            tiles_cut = [0]

            def cut_tile():
                t = tiles_cut[0]
                tiles_cut[0] += 1
                dve.wait_ge(exp3_done, t + 1)
                p = rows[:, E3_BUF[t], 0:M]
                link(dve.scalar_tensor_tensor(out=p, in0=rows[:, S3_BUF[t], 0:M], scalar=thr3[:, t:t + 1], in1=p,
                                              op0=ALU.is_ge, op1=ALU.mult, accum_out=sum3[:, t:t + 1]))
                dve.reciprocal(r3[:, t:t + 1], sum3[:, t:t + 1]).then_inc(p3_ready, 1)

            def topk_some(n):
                for _ in range(n):
                    if topk_at[0] < NT // 2 - 1:
                        got = next(topk)
                        if got is not None:
                            topk_at[0] = got

            def topk_tile(t):
                while topk_at[0] < t:
                    got = next(topk, NT)
                    if got is not None:
                        topk_at[0] = got

            topk_at = [-1]

            dve.wait_ge(fixed_in, 48)
            dve.wait_ge(consts, 4 + E)
            for i in range(2):
                raw = rows[:, 6 + i, 0:KC * D].rearrange("p (k d) -> p k d", k=KC)
                link(dve.tensor_copy(fixed_hi[:, i, :, :], raw))
                dve.tensor_tensor(fixed_lo[:, i, :, :], raw, fixed_hi[:, i, :, :].bitcast(F32), ALU.subtract)
            dve.tensor_copy(wr_hi[:, :, :], wr_raw[:, :, :]).then_inc(wr_split, 1)
            dve.wait_ge(wr_split, 1)
            dve.tensor_tensor(wr_lo[:, :, :], wr_raw[:, :, :], wr_hi[:, :, :].bitcast(F32), ALU.subtract) \
               .then_inc(wr_split, 1)

            hidden = 0
            s1_freed = [0, 0]
            for step in STEPS:
                kind = step[0]
                if kind == "ln":
                    normalise(step)
                elif kind == "xT":
                    q = step[1]
                    t_lo_out(step, xT_lo[:, q % NXT, :, :].rearrange("p k s -> p (k s)"), t_bank(step)[:, :],
                             xT_hi[:, q % NXT, :, :].rearrange("p k s -> p (k s)"))
                elif kind == "scores1":
                    b = step[1]
                    dve.wait_ge(mask_ready, b + 1)
                    for c, (c0, w) in enumerate(KCHUNKS):
                        w = min(w, M - c0)
                        for i in range(TB):
                            t = 2 * b + i
                            key = ("s1", t, c)
                            if c == 0 and t >= 4:
                                dve.wait_ge(t_ready, T_UNIT[("p1", 0 if t < 6 else 2, NU - 1)] + 1)
                            dve.wait_ge(s_ready, S_UNIT[key] + 1)
                            last = dve.tensor_tensor_reduce(out=rows[:, S1_BUF[t], c0:c0 + w], in0=s_bank(key)[:, 0:w],
                                                     in1=mask_add[:, c0:c0 + w], scale=1.0, scalar=BELOW_ALL,
                                                     op0=ALU.add, op1=ALU.max, accum_out=mx1c[:, i, c:c + 1])
                            last.then_inc(s_free[S_UNIT[key] % 2], 1)
                            s1_freed[S_UNIT[key] % 2] += 1
                        if b >= 2:
                            topk_some(1)
                    for n in range(2):
                        dve.wait_ge(s_free[n], s1_freed[n])
                    link(dve.tensor_reduce(mx1[:, 2 * b:2 * b + 2], mx1c[:, :, :], AX.X, ALU.max))
                    dve.tensor_scalar(nm1[:, 2 * b:2 * b + 2], mx1[:, 2 * b:2 * b + 2], -SCALE, None, ALU.mult) \
                       .then_inc(max1_ready, 2)
                elif kind in ("pv1", "pv3"):
                    b, s = step[1], kind[-1]
                    if kind == "pv3":
                        for t in (2 * b, 2 * b + 1):
                            if tiles_cut[0] <= t:
                                topk_tile(t)
                                cut_tile()
                    for u, mcs in enumerate(UNITS):
                        key = ("p" + s, b, u)
                        slot = P_UNIT[key] % NPT
                        r, w = MROWS[mcs[-1]], len(mcs) * TB * P
                        t_lo_out(key, pT_lo[0:r, slot, :, :, :].rearrange("p a i s -> p (a i s)")[:, 0:w],
                                 t_bank(key)[0:r, 0:w],
                                 pT_hi[0:r, slot, :, :, :].rearrange("p a i s -> p (a i s)")[:, 0:w])
                        if b >= 2 and kind == "pv1" and u % 2 == 1:
                            topk_some(1)
                    if kind == "pv1":
                        t0 = 2 * b
                        dve.wait_ge(exp1_done, t0 + 2)
                        link(dve.reciprocal(r1[:, t0:t0 + 2], sum1[:, t0:t0 + 2]))
                        link(dve.scalar_tensor_tensor(out=r1[:, t0:t0 + 2], in0=mx1[:, t0:t0 + 2], scalar=NEG / 16,
                                                      in1=r1[:, t0:t0 + 2], op0=ALU.is_gt, op1=ALU.mult))
                        dve.wait_ge(x_in[b], 16)
                        for t in (t0, t0 + 1):
                            key = ("pv1", t)
                            dve.wait_ge(o_ready, O_UNIT[key] + 1)
                            dve.scalar_tensor_tensor(out=x_res[:, t, :], in0=o_bank(key)[:, 0:D], scalar=r1[:, t:t + 1],
                                                     in1=x_res[:, t, :], op0=ALU.mult, op1=ALU.add).then_inc(o_out, 1)
                    else:
                        slot = QA_USE[("aT", b)] % NQA
                        for d in range(KC):
                            key = ("aT", b, d)
                            dve.wait_ge(o_hi, O_SPLIT[key] + 1)
                            dve.tensor_tensor(qa_lo[:, slot, d, :], o_bank(key)[:, 0:S],
                                              qa_hi[:, slot, d, :].bitcast(F32), ALU.subtract).then_inc(o_out, 1)
                elif kind == "router":
                    dve.wait_ge(o_ready, O_UNIT[step] + 1)
                    if step[1]:
                        dve.wait_ge(o_out, O_UNIT[("down", 0, E - 1, 3)] + 1)
                    link(dve.tensor_copy(logits[:, :, :].rearrange("p t e -> p (t e)"), o_bank(step)[:, 0:4 * E]))
                    for t in range(4):
                        last = dve.max(top8[:, t, :], logits[:, t, :])
                    link(last)
                    dve.tensor_tensor(gap[:, :], top8[:, :, 1], top8[:, :, 0], ALU.subtract).then_inc(gap_ready, 1)
                    for t in range(4):
                        last = dve.max_index(idx8[:, t, :], top8[:, t, :], logits[:, t, :])
                    link(last)
                    link(dve.tensor_copy(idxf[:, :, :], idx8[:, :, :]))
                    dve.wait_ge(egap_ready, step[1] + 1)
                    link(dve.tensor_scalar(w_top[:, 1, :], egap[:, :], 1.0, None, ALU.add))
                    link(dve.reciprocal(w_top[:, 0, :], w_top[:, 1, :]))
                    link(dve.tensor_tensor(w_top[:, 1, :], egap[:, :], w_top[:, 0, :], ALU.mult))
                    for t in range(4):
                        dve.tensor_scalar(w_tmp[:, t, :], iota8[:, :], idxf[:, t, 0:1], w_top[:, 0, t:t + 1],
                                          ALU.is_equal, ALU.mult)
                        last = dve.tensor_scalar(w_sel[:, t, :], iota8[:, :], idxf[:, t, 1:2], w_top[:, 1, t:t + 1],
                                                 ALU.is_equal, ALU.mult)
                    link(last)
                    last = dve.tensor_tensor(w_sel[:, :, :], w_sel[:, :, :], w_tmp[:, :, :], ALU.add)
                    last.then_inc(o_out, 1)
                    dve.wait_ge(o_out, O_UNIT[step] + 1)
                elif kind == "gu":
                    j = hidden
                    hidden += 1
                    dve.wait_ge(silu_done, j + 1)
                    dve.wait_ge(u_ready, j + 1)
                    dve.tensor_tensor(hid[:, j % 2, :], hid[:, j % 2, :], U_bank[:, :], ALU.mult).then_inc(hid_done, 1)
                    if step[1] == 1:
                        topk_some(1)
                elif kind == "down":
                    _, h, e = step
                    for i in range(4):
                        key = (*step, i)
                        t = 4 * h + i
                        dve.wait_ge(o_ready, O_UNIT[key] + 1)
                        if e:
                            dve.wait_ge(o_out, O_UNIT[("down", h, e - 1, i)] + 1)
                        dve.scalar_tensor_tensor(out=x_res[:, t, :], in0=o_bank(key)[:, 0:D],
                                                 scalar=w_sel[:, i, e:e + 1], in1=x_res[:, t, :],
                                                 op0=ALU.mult, op1=ALU.add).then_inc(o_out, 1)
                    if h == 1:
                        topk_some(1)
                elif kind == "coef":
                    dve.wait_ge(coef_e, 2)
                    col = lambda c: scal[:, c:c + 1]
                    link(dve.tensor_scalar(col(6), col(4), 1.0, None, ALU.add))
                    link(dve.reciprocal(col(7), col(6)))
                    link(dve.tensor_scalar(col(8), col(7), -1.0, 1.0, ALU.mult, ALU.add))
                    link(dve.tensor_tensor(col(8), col(8), col(1), ALU.mult))
                    link(dve.scalar_tensor_tensor(out=col(9), in0=col(0), scalar=col(7), in1=col(8),
                                                  op0=ALU.mult, op1=ALU.add))
                    link(dve.tensor_scalar(col(10), col(9), SCALE, None, ALU.mult))
                    dve.tensor_tensor(col(11), col(10), col(5), ALU.mult).then_inc(coef_ready, 1)
                elif kind == "wquant":
                    which = step[1]
                    n = which - 1
                    if which == 1:
                        link(dve.memset(wabs[:, :], 0.0))
                    dve.wait_ge(wq_in, 16 * which)
                    dve.tensor_reduce(wabs[:, n:n + 1], w_raw, AX.X, ALU.add, apply_absolute_value=True) \
                       .then_inc(wabs_ready, 1)
                    dve.wait_ge(o_ready, O_UNIT[step] + 1)
                    dve.tensor_scalar(wdeq[:, n:n + 1], o_bank(step)[:, n:n + 1], 1.0 / (D * H4), EPS,
                                      ALU.mult, ALU.max).then_inc(o_out, 1)
                    dve.wait_ge(o_out, O_UNIT[step] + 1)
                    link(dve.reciprocal(wscl[:, n:n + 1], wdeq[:, n:n + 1]))
                    link(dve.tensor_scalar(w_raw, w_raw, wscl[:, n:n + 1], MAGIC, ALU.mult, ALU.add))
                    link(dve.tensor_scalar(w_raw, w_raw, MAGIC, 1.0, ALU.subtract, ALU.min))
                    dve.tensor_scalar(w_views[which][1][:, :, :].rearrange("p k n -> p (k n)"), w_raw, -1.0, None,
                                      ALU.max).then_inc(w_done, 1)
                elif kind == "qT":
                    use = QA_USE[step]
                    dve.wait_ge(o_hi, O_SPLIT[step] + 1)
                    flat = lambda v: v[:, use % NQA, :, :].rearrange("p k s -> p (k s)")
                    dve.scalar_tensor_tensor(out=flat(qa_lo), in0=o_bank(step)[:, :], scalar=scal[:, 11:12],
                                             in1=flat(qa_hi).bitcast(F32), op0=ALU.mult, op1=ALU.subtract) \
                       .then_inc(o_out, 1)
                elif kind == "wo":
                    b = step[1]
                    for t in (2 * b, 2 * b + 1):
                        key = ("wo", t)
                        dve.wait_ge(o_ready, O_UNIT[key] + 1)
                        dve.wait_ge(p3_ready, t + 1)
                        dve.scalar_tensor_tensor(out=x_res[:, t, :], in0=o_bank(key)[:, 0:D], scalar=r3[:, t:t + 1],
                                                 in1=x_res[:, t, :], op0=ALU.mult, op1=ALU.add).then_inc(o_out, 1)
                elif kind == "ln4":
                    b = step[1]
                    normalise(step)
                    link(dve.tensor_reduce(xmx[:, :], xn[:, :, :], AX.X, ALU.max, apply_absolute_value=True))
                    link(dve.tensor_scalar(xmx[:, :], xmx[:, :], EPS, None, ALU.max))
                    link(dve.reciprocal(xinv[:, :], xmx[:, :]))
                    link(dve.tensor_scalar(xscl[:, :], xinv[:, :], 127.0, None, ALU.mult))
                    if b:
                        dve.wait_ge(gelu_done, 4 * b)
                    link(dve.tensor_scalar(xdeq[:, :], xmx[:, :], wdeq[:, 0:1], 1.0 / 127.0, ALU.mult, ALU.mult))
                    if b:
                        dve.wait_ge(t_ready, T_UNIT[("q4", b - 1)] + 1)
                    for i in range(TB):
                        last = dve.tensor_scalar(xn[:, i, :], xn[:, i, :], xscl[:, i:i + 1], MAGIC, ALU.mult, ALU.add)
                    link(last)
                    dve.tensor_scalar(xq[:, :, :], xn[:, :, :], MAGIC, -128.0, ALU.subtract, ALU.max) \
                       .then_inc(xq_ready, 1)
                elif kind == "q4":
                    dve.wait_ge(t_ready, T_UNIT[step] + 1)
                    if step[1]:
                        dve.wait_ge(s_ready, S_UNIT[("up4", 2 * step[1] - 1, 1)] + 1)
                    dve.tensor_scalar(xqT[:, :, :, :].rearrange("p k i s -> p (k i s)"),
                                      t_bank(step)[:, :].bitcast(BF16)[:, 0:512], 127.0, None, ALU.min) \
                       .then_inc(t_out, 1)
                elif kind == "up4":
                    t = step[1]
                    dve.wait_ge(gelu_done, 2 * t + 2)
                    link(dve.tensor_reduce(gmx[:, :], gel[:, :], AX.X, ALU.max, apply_absolute_value=True))
                    link(dve.tensor_scalar(gmx[:, :], gmx[:, :], EPS, None, ALU.max))
                    link(dve.reciprocal(ginv[:, :], gmx[:, :]))
                    link(dve.tensor_scalar(gscl[:, :], ginv[:, :], 127.0, None, ALU.mult))
                    link(dve.tensor_scalar(gdeq[:, :], gmx[:, :], wdeq[:, 1:2], 1.0 / 127.0, ALU.mult, ALU.mult))
                    link(dve.tensor_scalar(gel[:, :], gel[:, :], gscl[:, :], MAGIC, ALU.mult, ALU.add))
                    if t:
                        dve.wait_ge(t_ready, T_UNIT[("h4T", t - 1)] + 1)
                    dve.tensor_scalar(gel_q[:, :], gel[:, :], MAGIC, -128.0, ALU.subtract, ALU.max) \
                       .then_inc(gelq_ready, 1)
                elif kind == "h4T":
                    t = step[1]
                    dve.wait_ge(t_ready, T_UNIT[step] + 1)
                    if t:
                        dve.wait_ge(o_ready, O_UNIT[("down4", t - 1)] + 1)
                    dve.tensor_scalar(gelT[:, :], t_bank(step)[:, :].bitcast(BF16), 127.0, None, ALU.min) \
                       .then_inc(t_out, 1)
                elif kind == "down4":
                    t = step[1]
                    dve.wait_ge(o_ready, O_UNIT[step] + 1)
                    wait(dve, stored, 16 * t)
                    dve.scalar_tensor_tensor(out=fin[:, :], in0=o_bank(step)[:, 0:D], scalar=gdeq[:, :],
                                             in1=x_res[:, t, :], op0=ALU.mult, op1=ALU.add).then_inc(fin_ready, 1)
                    dve.wait_ge(fin_ready, t + 1)
                    dve.sem_inc(o_out, 1)


def owner(key):
    if key[0] in ("p1", "p3"):
        return ("pv" + key[0][1], key[1])
    if key[0] in ("pv1",):
        return ("pv1", key[1] // 2)
    if key[0] == "aT":
        return ("pv3", key[1])
    if key[0] == "wo":
        return ("wo", key[1] // 2)
    if key[0] == "down":
        return key[:3]
    return key


def kernel(**inputs):
    import concourse.bacc as bacc
    from concourse.bass_utils import run_bass_kernel_spmd

    a = {k: np.asarray(v) for k, v in inputs.items()}
    arrays = {
        "x": a["x"].reshape(B * S, D),
        "ctx": a["ctx_2048"],
        "ctxT": a["ctx_2048"].transpose(0, 2, 1),
        "mask": a["mask_BxS2_bk0"].reshape(-1).view(np.uint32),
        "Wr": a["L0_ffn_Wr"], "Wg": a["L0_ffn_Wg"], "Wu": a["L0_ffn_Wu"], "Wd": a["L0_ffn_Wd"],
        "WqT": a["L1_xattn_W_qkv"][:D].T, "WoT": a["L1_xattn_W_o"].T,
        "beta_q": a["L1_xattn_beta_q"].reshape(1, 1), "beta_k": a["L1_xattn_beta_k"].reshape(1, 1),
        "gate": a["L1_xattn_gate"].reshape(1, 1), "log_tau": a["L1_xattn_log_tau"].reshape(1, 1),
        "w1T": a["L1_ffn_w1"].T, "w2T": a["L1_ffn_w2"].T,
    }
    arrays = {k: np.ascontiguousarray(v) for k, v in arrays.items()}
    nc = bacc.Bacc("TRN2", target_bir_lowering=False, num_devices=1)
    args = [nc.dram_tensor(k, v.shape, mybir.dt.from_np(v.dtype), kind="ExternalInput").ap()
            for k, v in arrays.items()]
    out = nc.dram_tensor("out", (B * S, D), F32, kind="ExternalOutput").ap()
    two_layers(nc, *args, out)
    r = run_bass_kernel_spmd(nc, [arrays], core_ids=[0])
    return r.results[0]["out"].reshape(B, S, D)
```
